# Optimizing a Trainium2 kernel written in Bass

```python
import numpy as np
import jax
import jax.numpy as jnp

def _softmax(x, axis=-1):
    return jax.nn.softmax(x, axis=axis)

def _gelu(x):
    return jax.nn.gelu(x, approximate=True)

def _silu(x):
    return jax.nn.silu(x)

def _sigmoid(x):
    return jax.nn.sigmoid(x)

def _layernorm(x, axis=-1, eps=1e-05):
    m = jnp.mean(x, axis=axis, keepdims=True)
    v = jnp.var(x, axis=axis, keepdims=True)
    return (x - m) / jnp.sqrt(v + eps)

def _scatter_add(tgt, idx, src, axis=0):
    return tgt.at[idx].add(src)

def _segment_sum(src, seg, n):
    return jax.ops.segment_sum(src, seg, n)
kernel_name = 'mk_prb_d2_jaxref_r8_6accdf'

def setup_inputs(seed: int=0):
    np.random.seed(seed)
    _w = jnp.asarray

    def _L0_attn_setup():
        import jax, jax.numpy as jnp
        import numpy as np
        D_MODEL = 256
        N_HEADS = 16
        HEAD_DIM = D_MODEL // N_HEADS
        SCALE = HEAD_DIM ** (-0.5)
        key = jax.random.key(seed)
        ks = jax.random.split(key, 9)
        B, L, D = (4, 512, D_MODEL)
        s = 1.0 / np.sqrt(D)
        inp = {'x': jax.random.normal(ks[0], (B, L, D), dtype=jnp.float32)}
        inp['Wq'] = jax.random.normal(ks[1], (D, D), dtype=jnp.float32) * s
        inp['bq'] = jnp.zeros((D,), dtype=jnp.float32)
        inp['Wk'] = jax.random.normal(ks[2], (D, D), dtype=jnp.float32) * s
        inp['bk'] = jnp.zeros((D,), dtype=jnp.float32)
        inp['Wv'] = jax.random.normal(ks[3], (D, D), dtype=jnp.float32) * s
        inp['bv'] = jnp.zeros((D,), dtype=jnp.float32)
        inp['Wo'] = jax.random.normal(ks[4], (D, D), dtype=jnp.float32) * s
        inp['bo'] = jnp.zeros((D,), dtype=jnp.float32)
        return inp
    _L0_attn_in = _L0_attn_setup()

    def _L0_ffn_setup():
        import jax, jax.numpy as jnp
        import numpy as np
        N_ACTIVE = 32
        key = jax.random.key(seed)
        ks = jax.random.split(key, 6)
        B, T, D, G, GD = (4, 256, 256, 512, 32)
        x = jax.random.normal(ks[0], (B, T, D), jnp.float32)
        Wc = jax.random.normal(ks[1], (G, D), jnp.float32) * D ** (-0.5)
        temperature = jnp.array(1.0, jnp.float32)
        genes = jax.random.normal(ks[2], (G, GD), jnp.float32) * 0.02
        Wd = jax.random.normal(ks[3], (D, GD), jnp.float32) * GD ** (-0.5)
        Wu = jax.random.normal(ks[4], (D, GD), jnp.float32) * 0.02
        norm_w = jnp.ones((D,), jnp.float32)
        scale = jnp.array(0.1, jnp.float32)
        return {'x': x, 'Wc': Wc, 'temperature': temperature, 'genes': genes, 'Wd': Wd, 'Wu': Wu, 'norm_w': norm_w, 'scale': scale}
    _L0_ffn_in = _L0_ffn_setup()

    def _L1_attn_setup():
        import jax, jax.numpy as jnp
        import numpy as np
        EPS = 1.1920929e-07

        def _rms(x):
            return x * jax.lax.rsqrt(jnp.mean(x * x, axis=-1, keepdims=True) + EPS)
        key = jax.random.key(seed)
        k0, k1, k2, k3 = jax.random.split(key, 4)
        B, S, D, DFF = (4, 256, 256, 1024)
        x = jax.random.normal(k0, (B, S, D), dtype=jnp.float32)
        w_qkv = jax.random.normal(k1, (3 * D, D), dtype=jnp.float32) * 0.02
        w_swiglu = jax.random.normal(k2, (2 * DFF, D), dtype=jnp.float32) * 0.02
        w_out = jax.random.normal(k3, (D, DFF), dtype=jnp.float32) * 0.02
        return {'x': x, 'w_qkv': w_qkv, 'w_swiglu': w_swiglu, 'w_out': w_out}
    _L1_attn_in = _L1_attn_setup()

    def _L1_ffn_setup():
        import jax, jax.numpy as jnp
        import numpy as np
        H = 256
        I = 176
        E = 16
        K = 2
        SI = I * 2

        def _swiglu(gu, inter):
            g, u = (gu[..., :inter], gu[..., inter:])
            return jax.nn.silu(g) * u
        key = jax.random.key(seed)
        ks = jax.random.split(key, 6)
        s = 0.02
        hidden_states = jax.random.normal(ks[0], (1, 128, H), dtype=jnp.float32)
        gate_w = jax.random.normal(ks[1], (E, H), dtype=jnp.float32) * s
        w_gate_up = jax.random.normal(ks[2], (E, H, 2 * I), dtype=jnp.float32) * s
        w_down = jax.random.normal(ks[3], (E, I, H), dtype=jnp.float32) * s
        shared_gate_up = jax.random.normal(ks[4], (H, 2 * SI), dtype=jnp.float32) * s
        shared_down = jax.random.normal(ks[5], (SI, H), dtype=jnp.float32) * s
        return {'hidden_states': hidden_states, 'gate_w': gate_w, 'w_gate_up': w_gate_up, 'w_down': w_down, 'shared_gate_up': shared_gate_up, 'shared_down': shared_down}
    _L1_ffn_in = _L1_ffn_setup()
    _d = {'L0_attn_x': _L0_attn_in['x'], 'L0_attn_Wq': _L0_attn_in['Wq'], 'L0_attn_bq': _L0_attn_in['bq'], 'L0_attn_Wk': _L0_attn_in['Wk'], 'L0_attn_bk': _L0_attn_in['bk'], 'L0_attn_Wv': _L0_attn_in['Wv'], 'L0_attn_bv': _L0_attn_in['bv'], 'L0_attn_Wo': _L0_attn_in['Wo'], 'L0_attn_bo': _L0_attn_in['bo'], 'L0_ffn_Wc': _L0_ffn_in['Wc'], 'L0_ffn_temperature': _L0_ffn_in['temperature'], 'L0_ffn_genes': _L0_ffn_in['genes'], 'L0_ffn_Wd': _L0_ffn_in['Wd'], 'L0_ffn_Wu': _L0_ffn_in['Wu'], 'L0_ffn_norm_w': _L0_ffn_in['norm_w'], 'L0_ffn_scale': _L0_ffn_in['scale'], 'L1_attn_w_qkv': _L1_attn_in['w_qkv'], 'L1_attn_w_swiglu': _L1_attn_in['w_swiglu'], 'L1_attn_w_out': _L1_attn_in['w_out'], 'L1_ffn_gate_w': _L1_ffn_in['gate_w'], 'L1_ffn_w_gate_up': _L1_ffn_in['w_gate_up'], 'L1_ffn_w_down': _L1_ffn_in['w_down'], 'L1_ffn_shared_gate_up': _L1_ffn_in['shared_gate_up'], 'L1_ffn_shared_down': _L1_ffn_in['shared_down']}
    _x0 = _d['L0_attn_x']
    _d['L0_attn_x'] = jax.random.normal(jax.random.fold_in(jax.random.key(seed), 1), (4, 512, 256), dtype=_x0.dtype)
    del _x0
    return _d

def reference(L0_attn_x, L0_attn_Wq, L0_attn_bq, L0_attn_Wk, L0_attn_bk, L0_attn_Wv, L0_attn_bv, L0_attn_Wo, L0_attn_bo, L0_ffn_Wc, L0_ffn_temperature, L0_ffn_genes, L0_ffn_Wd, L0_ffn_Wu, L0_ffn_norm_w, L0_ffn_scale, L1_attn_w_qkv, L1_attn_w_swiglu, L1_attn_w_out, L1_ffn_gate_w, L1_ffn_w_gate_up, L1_ffn_w_down, L1_ffn_shared_gate_up, L1_ffn_shared_down):

    def _L0_attn_ref(x, Wq, bq, Wk, bk, Wv, bv, Wo, bo):
        import jax, jax.numpy as jnp
        import numpy as np
        D_MODEL = 256
        N_HEADS = 16
        HEAD_DIM = D_MODEL // N_HEADS
        SCALE = HEAD_DIM ** (-0.5)
        B, L, D = x.shape
        H, Hd = (N_HEADS, HEAD_DIM)
        q = jnp.einsum('bld,ed->ble', x, Wq) + bq
        k = jnp.einsum('bld,ed->ble', x, Wk) + bk
        v = jnp.einsum('bld,ed->ble', x, Wv) + bv
        phi_q = jax.nn.elu(q) + 1.0
        phi_k = jax.nn.elu(k) + 1.0
        phi_q = phi_q.reshape(B, L, H, Hd)
        phi_k = phi_k.reshape(B, L, H, Hd)
        v = v.reshape(B, L, H, Hd)
        kv_sum = jnp.cumsum(phi_k * v, axis=1)
        context = (phi_q * kv_sum).reshape(B, L, D) * SCALE
        return jnp.einsum('bld,ed->ble', context, Wo) + bo

    def _L0_ffn_ref(x, Wc, temperature, genes, Wd, Wu, norm_w, scale):
        import jax, jax.numpy as jnp
        import numpy as np
        N_ACTIVE = 32
        eps = jnp.finfo(x.dtype).eps
        xn = x * jax.lax.rsqrt(jnp.mean(x * x, axis=-1, keepdims=True) + eps) * norm_w
        logits = jnp.einsum('btd,gd->btg', xn, Wc) / jnp.clip(temperature, 0.1)
        top_vals, top_idx = jax.lax.top_k(logits, N_ACTIVE)
        expr_w = jax.nn.softmax(top_vals, axis=-1)
        expressed = jnp.einsum('btk,btkc->btc', expr_w, genes[top_idx])
        down = jnp.tanh(jnp.einsum('btc,dc->btd', expressed, Wd))
        up = jnp.einsum('btc,dc->btd', expressed, Wu)
        return down * xn * up * scale

    def _L1_attn_ref(x, w_qkv, w_swiglu, w_out):
        import jax, jax.numpy as jnp
        import numpy as np
        EPS = 1.1920929e-07

        def _rms(x):
            return x * jax.lax.rsqrt(jnp.mean(x * x, axis=-1, keepdims=True) + EPS)
        qkv = _rms(x) @ w_qkv.T
        q, k, v = jnp.split(qkv, 3, axis=-1)
        q = _rms(q)
        k = _rms(k)
        w = jnp.exp(k)
        kv_cum = jnp.cumsum(w * v, axis=1)
        w_cum = jnp.cumsum(w, axis=1)
        y = jax.nn.sigmoid(q) * (kv_cum / (w_cum + 1e-06))
        uv = y @ w_swiglu.T
        u, g = jnp.split(uv, 2, axis=-1)
        return x + u * jax.nn.silu(g) @ w_out.T

    def _L1_ffn_ref(hidden_states, gate_w, w_gate_up, w_down, shared_gate_up, shared_down):
        import jax, jax.numpy as jnp
        import numpy as np
        H = 256
        I = 176
        E = 16
        K = 2
        SI = I * 2

        def _swiglu(gu, inter):
            g, u = (gu[..., :inter], gu[..., inter:])
            return jax.nn.silu(g) * u
        orig_shape = hidden_states.shape
        x = hidden_states.reshape(-1, H)
        logits = jnp.einsum('th,eh->te', x, gate_w)
        scores = jax.nn.softmax(logits, axis=-1)
        topk_w, topk_idx = jax.lax.top_k(scores, K)
        combine = jnp.sum(jax.nn.one_hot(topk_idx, E, dtype=x.dtype) * topk_w[..., None], axis=1)
        gu = jnp.einsum('th,ehj->etj', x, w_gate_up)
        h = _swiglu(gu, I)
        y = jnp.einsum('eti,eih,te->th', h, w_down, combine)
        gu_s = x @ shared_gate_up
        y = y + _swiglu(gu_s, SI) @ shared_down
        return y.reshape(orig_shape)
    x = L0_attn_x
    xn = _layernorm(x, axis=-1)
    x = x + _L0_attn_ref(xn, L0_attn_Wq, L0_attn_bq, L0_attn_Wk, L0_attn_bk, L0_attn_Wv, L0_attn_bv, L0_attn_Wo, L0_attn_bo) + _L0_ffn_ref(xn, L0_ffn_Wc, L0_ffn_temperature, L0_ffn_genes, L0_ffn_Wd, L0_ffn_Wu, L0_ffn_norm_w, L0_ffn_scale)
    xn = _layernorm(x, axis=-1)
    x = x + _L1_attn_ref(xn, L1_attn_w_qkv, L1_attn_w_swiglu, L1_attn_w_out) + _L1_ffn_ref(xn, L1_ffn_gate_w, L1_ffn_w_gate_up, L1_ffn_w_down, L1_ffn_shared_gate_up, L1_ffn_shared_down)
    return x

_drawn_inputs = setup_inputs


def setup_inputs(seed=0):
    import zlib

    import numpy as np

    out = dict(_drawn_inputs(seed))
    spreads = {'L0_attn_bq': (0.0, 0.1),
     'L0_attn_bk': (0.0, 0.1),
     'L0_attn_bv': (0.0, 0.1),
     'L0_attn_bo': (0.0, 0.8),
     'L0_ffn_norm_w': (1.0, 0.6)}
    factors = {'L0_ffn_Wc': 64.0,
     'L0_ffn_genes': 64.0,
     'L0_ffn_Wd': 64.0,
     'L0_ffn_Wu': 64.0,
     'L1_attn_w_qkv': 8.0,
     'L1_attn_w_swiglu': 8.0,
     'L1_attn_w_out': 8.0,
     'L1_ffn_gate_w': 8.0,
     'L1_ffn_w_gate_up': 8.0,
     'L1_ffn_w_down': 8.0,
     'L1_ffn_shared_gate_up': 8.0,
     'L1_ffn_shared_down': 8.0}
    for name, (base, spread) in spreads.items():
        noise = np.random.default_rng([zlib.crc32(name.encode()), seed]).standard_normal(out[name].shape)
        drawn = base * np.exp(spread * noise) if base else spread * noise
        out[name] = jnp.asarray(drawn.astype(out[name].dtype))
    for name, factor in factors.items():
        out[name] = (out[name] * factor).astype(out[name].dtype)
    return out
```

```python
from contextlib import ExitStack

import numpy as np

import concourse.bass as bass
from concourse import mybir

F32 = mybir.dt.float32
U32 = mybir.dt.uint32
ALU = mybir.AluOpType
ACT = mybir.ActivationFunctionType
AX = mybir.AxisListType.X

P = 128
NB = 4
T = 512
D = 256
NT = T // P
E = 16
EPS = 2.0 ** -23
LN_EPS = 1e-5
LOWEST = -3.4e38

V_BQ, V_BK, V_BV, V_BO, V_NW, V_SC, V_TP = 0, 2, 4, 6, 8, 10, 11
C_LN, C_LNR, C_RMS = 0, 1, 2


class Queue:

    def __init__(self, sem):
        self.sem, self.n, self.ops, self.seen = sem, 0, [], {}

    def wait(self, *tokens):
        for t in tokens:
            if t is None:
                continue
            sem, value = t
            if self.seen.get(id(sem), 0) < value:
                self.seen[id(sem)] = value
                self.ops.append(lambda e, s=sem, v=value: e.wait_ge(s, v))

    def do(self, waits, fn, *args, **named):
        self.wait(*waits)
        self.n += 1
        self.ops.append(lambda e: fn(*args, **named).then_inc(self.sem, 1))
        return (self.sem, self.n)

    def run(self, waits, fn, *args, **named):
        self.wait(*waits)
        self.ops.append(lambda e: fn(*args, **named))

    def dma(self, out, in_, sem, count, *waits):
        self.wait(*waits)
        self.ops.append(lambda e: e.dma_start(out, in_).then_inc(sem, 16))
        return (sem, 16 * count)

    def play(self, e):
        for op in self.ops:
            op(e)


class Place:

    def __init__(self, t):
        self.t, self.free, self.held = t, [], False

    def done(self, *tokens):
        assert self.held
        self.free, self.held = list(tokens), False


class Ring:
    def __init__(self, tensors):
        self.order = [Place(t) for t in tensors]

    def take(self):
        for i, p in enumerate(self.order):
            if not p.held:
                self.order.append(self.order.pop(i))
                p.held = True
                return p
        raise AssertionError("every place is held")


def build(nc, x, vec, cst, wqkv0, wo0, wc, genes, wdu, wqkv1, wsg, wout, gate, sgu, sdn, gu, dn, out):
    with ExitStack() as ctx:
        def sb(name, shape, dt=F32):
            return ctx.enter_context(nc.sbuf_tensor(name, shape, dt))

        def sem(name):
            return ctx.enter_context(nc.semaphore(name))

        pe, act, dve, pool, sp = (Queue(sem(f"s_{n}")) for n in ("pe", "act", "dve", "pool", "sp"))

        banks = Ring([ctx.enter_context(nc.psum_tensor(f"bank{i}", [P, 512], F32)) for i in range(8)])
        slots = Ring([sb(f"slot{i}", [P, 2, T]) for i in range(18)])

        W = {}
        for name, ap, shape in (
            ("cst", cst, [P, 8 + 2 * P + 16]), ("vec", vec, [P, 12]),
            ("wqkv0", wqkv0, [P, 2, 768]), ("wc", wc, [P, 2, 512]), ("wo0", wo0, [P, 2, D]),
            ("genes", genes, [P, 4, 64]), ("wdu", wdu, [32, 512]),
            ("wqkv1", wqkv1, [P, 2, 768]), ("gate", gate, [P, 2, E]), ("wsg", wsg, [P, 2, 2048]), ("sgu", sgu, [P, 2, 704]),
            ("wout", wout, [P, 8, D]), ("sdn", sdn, [88, 4, D]),
        ):
            W[name] = (sb("w_" + name, shape), sem("d_" + name), ap)

        def w(name):
            return W[name][0]

        def arrived(name):
            return (W[name][1], 16)

        xs = [sb(f"x{i}", [P, 2, T]) for i in range(2)]
        s_x = [sem(f"d_x{i}") for i in range(2)]
        ob = [sb(f"ob{i}", [P, NT, D]) for i in range(2)]
        s_out = [sem(f"d_out{i}") for i in range(2)]
        mg = [sb(f"mg{i}", [P, 2, 352]) for i in range(2)]
        md = [sb(f"md{i}", [88, 2, D]) for i in range(2)]
        s_mg = [sem(f"d_mg{i}") for i in range(2)]
        s_md = [sem(f"d_md{i}") for i in range(2)]
        sg = [sb(f"sg{i}", [P, 176]) for i in range(4)]
        hh = [sb(f"hh{i}", [P, 176]) for i in range(4)]
        hT = [sb(f"hT{i}", [88, 2, P]) for i in range(4)]
        ex = Ring([sb(f"ex{i}", [32, 2, T]) for i in range(1)])
        small = sb("small", [P, 16])
        m8 = sb("m8", [P, 4, 8])
        nb = sb("nb", [P, 1])
        g_m = sb("g_m", [P, 4])
        g_l = sb("g_l", [P, 4, E])
        g_s = sb("g_s", [P, 4, E])
        g_8 = sb("g_8", [P, 4, 8])
        g_i = sb("g_i", [P, 4, 8], U32)
        g_f = sb("g_f", [P, 4, 2])
        g_o = sb("g_o", [P, 2, 4, E])
        comb = sb("comb", [P, 4, E])

        c_t = w("cst")
        ident = c_t[:, 8:8 + P]
        mean = c_t[:, 8 + P:8 + 2 * P]
        iota = c_t[:, 8 + 2 * P:8 + 2 * P + 16]

        def col(i):
            return w("vec")[:, i:i + 1]

        def con(i):
            return c_t[:, i:i + 1]

        def load(name):
            t, s, ap = W[name]
            sp.dma(t[tuple(slice(None) for _ in t.shape)], ap, s, 1)

        load("cst")
        xtok = {0: sp.dma(xs[0][:, :, :], x[0], s_x[0], 1)}
        for n in W:
            if n != "cst":
                load(n)
            if n == "wc":
                xtok[1] = sp.dma(xs[1][:, :, :], x[1], s_x[1], 1)

        t_it = dve.do([arrived("vec")], nc.vector.tensor_scalar, small[:, 0:1], col(V_TP), 0.1, None, ALU.max)
        t_it = dve.do([t_it], nc.vector.reciprocal, small[:, 1:2], small[:, 0:1])
        t_it = dve.do([t_it], nc.vector.tensor_scalar, small[:, 2:3], small[:, 1:2], -1.0, None, ALU.mult)
        it, nit = small[:, 1:2], small[:, 2:3]

        def product(out_, terms, *waits):
            pe.wait(*waits)
            for i, (a, b) in enumerate(terms):
                first, last = i == 0, i == len(terms) - 1
                if last:
                    return pe.do([], nc.tensor.matmul, out_, a, b, start=first, stop=last)
                pe.run([], nc.tensor.matmul, out_, a, b, start=first, stop=last)

        def wide(ap):
            return ap[:, None, :].broadcast_to([P, 2, T])

        def norm(src, t_src):
            m = banks.take()
            t = product(m.t[:, :], [(mean, src[:, c, :]) for c in range(2)], arrived("cst"), *t_src, *m.free)
            xc = slots.take()
            t_xc = dve.do([t, *xc.free], nc.vector.tensor_tensor, xc.t[:, :, :], src, wide(m.t[:, :]), ALU.subtract)
            m.done(t_xc)
            sq = slots.take()
            t = act.do([t_xc, *sq.free], nc.scalar.activation, sq.t[:, :, :], xc.t[:, :, :], ACT.Square)
            v = banks.take()
            t = product(v.t[:, :], [(mean, sq.t[:, c, :]) for c in range(2)], t, *v.free)
            sq.done(t)
            r = slots.take()
            act.do([t, *r.free], nc.scalar.activation, r.t[:, 0, :], v.t[:, :], ACT.Ln, bias=con(C_LN))
            t = act.do([], nc.scalar.activation, r.t[:, 1, :], v.t[:, :], ACT.Ln, bias=con(C_LNR), scale=1.0 + EPS)
            v.done(t)
            t_r = act.do([t], nc.scalar.activation, r.t[:, :, :], r.t[:, :, :], ACT.Exp, scale=-0.5)
            return xc, t_xc, r, t_r

        def scan(dst, src, init, *waits):
            for c in range(2):
                t = dve.do([*waits], nc.vector.tensor_tensor_scan, dst[:, c, :], src[:, c, :], src[:, c, :], init, ALU.add, ALU.bypass)
            return t

        def layer0(b):
            src = xs[b % 2]
            xc, t_xc, r, t_r = norm(src[:, :, :], [xtok[b]])
            xn, xnn = slots.take(), slots.take()
            t_xn = dve.do([t_r, *xn.free], nc.vector.tensor_tensor, xn.t[:, :, :], xc.t[:, :, :], wide(r.t[:, 0, :]), ALU.mult)
            for c in range(2):
                t_xnn = dve.do([arrived("vec"), *xnn.free], nc.vector.scalar_tensor_tensor, xnn.t[:, c, :], xc.t[:, c, :], col(V_NW + c), r.t[:, 1, :], ALU.mult, ALU.mult)
            xc.done(t_xnn)
            r.done(t_xnn)

            def project(j, *waits):
                b_ = banks.take()
                t = product(b_.t[:, :], [(w("wqkv0")[:, c, j * P:(j + 1) * P], xn.t[:, c, :]) for c in range(2)],
                            arrived("wqkv0"), t_xn, *b_.free)
                return b_, t

            def phi(j0, bias):
                ph, rl = slots.take(), slots.take()
                for j in range(2):
                    b_, t = project(j0 + j)
                    act.do([t, arrived("vec"), *ph.free], nc.scalar.activation, ph.t[:, j, :], b_.t[:, :], ACT.Exp, bias=col(bias + j))
                    t = act.do([*rl.free], nc.scalar.activation, rl.t[:, j, :], b_.t[:, :], ACT.Relu, bias=col(bias + j))
                    b_.done(t)
                t = dve.do([t], nc.vector.scalar_tensor_tensor, ph.t[:, :, :], ph.t[:, :, :], 1.0, rl.t[:, :, :], ALU.min, ALU.add)
                rl.done(t)
                return ph, t

            phk, t_phk = phi(2, V_BK)
            pv = slots.take()
            for j in range(2):
                b_, t = project(4 + j)
                t_pv = dve.do([t, t_phk, *pv.free], nc.vector.scalar_tensor_tensor, pv.t[:, j, :], b_.t[:, :], col(V_BV + j), phk.t[:, j, :], ALU.add, ALU.mult)
                b_.done(t_pv)
            kv = slots.take()
            t_kv = scan(kv.t, pv.t, 0.0, t_pv, *kv.free)
            phk.done(t_pv)
            pv.done(t_kv)
            phq, t_phq = phi(0, V_BQ)
            xn.done((pe.sem, pe.n))
            t_ctx = dve.do([t_phq, t_kv], nc.vector.scalar_tensor_tensor, kv.t[:, :, :], phq.t[:, :, :], 0.25, kv.t[:, :, :], ALU.mult, ALU.mult)
            phq.done(t_ctx)
            yield

            et = [slots.take(), slots.take()]
            t_et = None
            for i in range(NT):
                b_ = banks.take()
                t = product(b_.t[:, :], [(xnn.t[:, c, i * P:(i + 1) * P], w("wc")[:, c, :]) for c in range(2)], arrived("wc"), t_xnn, *b_.free)
                wk, em = slots.take(), slots.take()
                wt = wk.t[:, 0, :]
                t = dve.do([t], nc.vector.max, m8[:, 0, :], b_.t[:, :])
                t1 = dve.do([t, t_it, act_last[0]], nc.vector.tensor_scalar, nb[:, :], m8[:, 0, 0:1], nit, None, ALU.mult)
                t = dve.do([*wk.free], nc.vector.match_replace, wt, m8[:, 0, :], b_.t[:, :], LOWEST)
                t_e = act.do([t1, t, *em.free], nc.scalar.activation, em.t[:, 0, :], b_.t[:, :], ACT.Exp, bias=nb[:, :], scale=it)
                act_last[0] = t_e
                b_.done(t_e)
                for k in range(1, 4):
                    t = dve.do([t], nc.vector.max, m8[:, k, :], wt)
                    t = dve.do([t], nc.vector.match_replace, wt, m8[:, k, :], wt, LOWEST)
                t = dve.do([t, t_e], nc.vector.scalar_tensor_tensor, em.t[:, 0, :], wt, LOWEST / 1.1, em.t[:, 0, :], ALU.is_le, ALU.mult)
                wk.done(t)
                b_ = banks.take()
                pe.wait(t, *b_.free)
                for g in range(4):
                    t = pe.do([], nc.tensor.transpose, b_.t[:, g * P:(g + 1) * P], em.t[:, 0, g * P:(g + 1) * P], ident)
                em.done(t)
                for h in range(2):
                    t_et = act.do([t, *et[h].free], nc.scalar.activation, et[h].t[:, :, i * P:(i + 1) * P], b_.t[:, h * 2 * P:(h + 1) * 2 * P].rearrange("p (g t) -> p g t", g=2), ACT.Copy)
                b_.done(t_et)
                yield
            b_ = banks.take()
            t = product(b_.t[0:64, :], [(w("genes")[:, g, :], et[g // 2].t[:, g % 2, :]) for g in range(4)], arrived("genes"), t_et, *b_.free)
            for s in et:
                s.done(t)
            x_ = ex.take()
            t = dve.do([t, *x_.free], nc.vector.reciprocal, x_.t[:, 0, :], b_.t[32:64, :])
            t_ex = dve.do([t], nc.vector.tensor_tensor, x_.t[:, 1, :], b_.t[0:32, :], x_.t[:, 0, :], ALU.mult)
            b_.done(t_ex)
            th, up = slots.take(), slots.take()
            for j in range(2):
                d_, u_ = banks.take(), banks.take()
                t = product(d_.t[:, :], [(w("wdu")[:, j * P:(j + 1) * P], x_.t[:, 1, :])], arrived("wdu"), t_ex, *d_.free)
                t_t = act.do([t, *th.free], nc.scalar.activation, th.t[:, j, :], d_.t[:, :], ACT.Tanh)
                d_.done(t_t)
                t = product(u_.t[:, :], [(w("wdu")[:, D + j * P:D + (j + 1) * P], x_.t[:, 1, :])], *u_.free)
                t_up = dve.do([t, t_t, *up.free], nc.vector.scalar_tensor_tensor, up.t[:, j, :], u_.t[:, :], col(V_SC), th.t[:, j, :], ALU.mult, ALU.mult)
                u_.done(t_up)
            x_.done(t)
            th.done(t_up)
            t_up = pool.do([t_up], nc.gpsimd.tensor_tensor, up.t[:, :, :], up.t[:, :, :], xnn.t[:, :, :], ALU.mult)
            xnn.done(t_up)
            x1 = slots.take()
            for j in range(2):
                b_ = banks.take()
                t = product(b_.t[:, :], [(w("wo0")[:, c, j * P:(j + 1) * P], kv.t[:, c, :]) for c in range(2)], arrived("wo0"), t_ctx, *b_.free)
                t1 = dve.do([t, t_up, *x1.free], nc.vector.scalar_tensor_tensor, x1.t[:, j, :], b_.t[:, :], col(V_BO + j), up.t[:, j, :], ALU.add, ALU.add)
                b_.done(t1)
            kv.done(t)
            up.done(t1)
            t1 = pool.do([t1], nc.gpsimd.tensor_tensor, x1.t[:, :, :], x1.t[:, :, :], src[:, :, :], ALU.add)
            if b + 2 < NB:
                xtok[b + 2] = sp.dma(src[:, :, :], x[b + 2], s_x[b % 2], 2, t1)
            res[b] = (x1, t1)
            yield

        act_last = [None]
        res, second = {}, {}
        ms = {"n": 0, "free": [[], []]}
        out_done = {}

        def layer1(b):
            x1, t_x1 = res[b]
            xc, t_xc, r, t_r = norm(x1.t[:, :, :], [t_x1])
            xn, xr = slots.take(), slots.take()
            t_xn = dve.do([t_r, *xn.free], nc.vector.tensor_tensor, xn.t[:, :, :], xc.t[:, :, :], wide(r.t[:, 0, :]), ALU.mult)
            t_xr = dve.do([*xr.free], nc.vector.tensor_tensor, xr.t[:, :, :], xc.t[:, :, :], wide(r.t[:, 1, :]), ALU.mult)
            xc.done(t_xr)
            r.done(t_xr)
            t_s = pool.do([t_xn, (pe.sem, pe.n)], nc.gpsimd.tensor_tensor, x1.t[:, :, :], x1.t[:, :, :], xn.t[:, :, :], ALU.add)
            yield

            b_ = banks.take()
            pe.wait(arrived("gate"), t_xn, *b_.free)
            for i in range(NT):
                t = product(b_.t[:, i * E:(i + 1) * E], [(xn.t[:, c, i * P:(i + 1) * P], w("gate")[:, c, :]) for c in range(2)])
            gl = b_.t[:, 0:NT * E].rearrange("p (i e) -> p i e", i=NT)
            t = dve.do([t], nc.vector.tensor_reduce, g_m[:, :], gl, AX, ALU.max)
            t = dve.do([t], nc.vector.tensor_tensor, g_l[:, :, :], gl, g_m[:, :, None].broadcast_to([P, NT, E]), ALU.subtract)
            b_.done(t)
            t = act.do([t], nc.scalar.activation, g_s[:, :, :], g_l[:, :, :], ACT.Exp)
            t = dve.do([t], nc.vector.tensor_reduce, g_m[:, :], g_s[:, :, :], AX, ALU.add)
            t = dve.do([t], nc.vector.reciprocal, g_m[:, :], g_m[:, :])
            t = dve.do([t], nc.vector.tensor_tensor, g_s[:, :, :], g_s[:, :, :], g_m[:, :, None].broadcast_to([P, NT, E]), ALU.mult)
            for i in range(NT):
                t1 = dve.do([t], nc.vector.max, g_8[:, i, :], g_s[:, i, :])
            for i in range(NT):
                t = dve.do([t1], nc.vector.max_index, g_i[:, i, :], g_8[:, i, :], g_s[:, i, :])
            t = dve.do([t], nc.vector.tensor_copy, g_f[:, :, :], g_i[:, :, 0:2])
            for k in range(2):
                t1 = dve.do([t], nc.vector.tensor_tensor, g_o[:, k, :, :], iota[:, None, :].broadcast_to([P, NT, E]), g_f[:, :, k:k + 1].broadcast_to([P, NT, E]), ALU.is_equal)
            for k in range(2):
                t = dve.do([t1], nc.vector.tensor_tensor, g_o[:, k, :, :], g_o[:, k, :, :], g_8[:, :, k:k + 1].broadcast_to([P, NT, E]), ALU.mult)
            t_comb = dve.do([t], nc.vector.tensor_tensor, comb[:, :, :], g_o[:, 0, :, :], g_o[:, 1, :, :], ALU.add)

            raw = []
            for j in range(4):
                b_ = banks.take()
                t = product(b_.t[:, :], [(w("wqkv1")[:, c, j * P:(j + 1) * P], xr.t[:, c, :]) for c in range(2)], arrived("wqkv1"), t_xr, *b_.free)
                raw.append((b_, t))
            hat = []
            for n in range(2):
                sq = slots.take()
                for j in range(2):
                    b_, t = raw[2 * n + j]
                    t_sq = act.do([t, *sq.free], nc.scalar.activation, sq.t[:, j, :], b_.t[:, :], ACT.Square)
                m = banks.take()
                t = product(m.t[:, :], [(mean, sq.t[:, c, :]) for c in range(2)], t_sq, *m.free)
                t = act.do([t], nc.scalar.activation, sq.t[:, 0, :], m.t[:, :], ACT.Ln, bias=con(C_RMS))
                m.done(t)
                t = act.do([t], nc.scalar.activation, sq.t[:, 0, :], sq.t[:, 0, :], ACT.Exp, scale=-0.5)
                h = slots.take()
                for j in range(2):
                    b_ = raw[2 * n + j][0]
                    t1 = dve.do([t, *h.free], nc.vector.tensor_tensor, h.t[:, j, :], b_.t[:, :], sq.t[:, 0, :], ALU.mult)
                    b_.done(t1)
                sq.done(t1)
                t1 = act.do([t1], nc.scalar.activation, h.t[:, :, :], h.t[:, :, :], ACT.Exp, scale=(-1.0, 1.0)[n])
                hat.append((h, t1))
            (eq, t_eq), (wk, t_wk) = hat
            wv = slots.take()
            for j in range(2):
                b_ = banks.take()
                t = product(b_.t[:, :], [(w("wqkv1")[:, c, (4 + j) * P:(5 + j) * P], xr.t[:, c, :]) for c in range(2)], *b_.free)
                t_wv = dve.do([t, t_wk, *wv.free], nc.vector.tensor_tensor, wv.t[:, j, :], b_.t[:, :], wk.t[:, j, :], ALU.mult)
                b_.done(t_wv)
            xr.done(t)
            kc, wc_ = slots.take(), slots.take()
            t_kc = scan(kc.t, wv.t, 0.0, t_wv, *kc.free)
            t_wc = scan(wc_.t, wk.t, 1e-6, *wc_.free)
            wv.done(t_kc)
            wk.done(t_wc)
            t = dve.do([t_eq, t_wc], nc.vector.scalar_tensor_tensor, eq.t[:, :, :], eq.t[:, :, :], 1.0, wc_.t[:, :, :], ALU.add, ALU.mult)
            t = dve.do([t], nc.vector.reciprocal, eq.t[:, :, :], eq.t[:, :, :])
            t_y = dve.do([t], nc.vector.tensor_tensor, kc.t[:, :, :], kc.t[:, :, :], eq.t[:, :, :], ALU.mult)
            wc_.done(t_y)
            eq.done(t_y)
            y = kc
            yield

            acc = [banks.take(), banks.take()]

            def add(i, lhsT, rhs, cols, first=False):
                a = acc[i // 2].t[:, (i % 2) * D + cols[0]:(i % 2) * D + cols[1]]
                return pe.do([], nc.tensor.matmul, a, lhsT, rhs, start=first, stop=False, skip_group_check=True)

            for a in acc:
                pe.wait(*a.free)
            pe.wait(t_s, arrived("cst"))
            for i in range(NT):
                for c in range(2):
                    t = add(i, x1.t[:, c, i * P:(i + 1) * P], ident, (c * P, c * P + P), first=(i % 2 == 0 and c == 0))
            x1.done(t)

            def swiglu(wname, oname, n, m, go, uo, src, t_src):
                g_, u_ = banks.take(), banks.take()
                t = product(g_.t[0:m, :], [(w(wname)[:, c, go + n * m:go + (n + 1) * m], src[:, c, :]) for c in range(2)], arrived(wname), t_src, *g_.free)
                s_ = slots.take()
                t_g = act.do([t, *s_.free], nc.scalar.activation, s_.t[0:m, 0, :], g_.t[0:m, :], ACT.Silu)
                g_.done(t_g)
                t = product(u_.t[0:m, :], [(w(wname)[:, c, uo + n * m:uo + (n + 1) * m], src[:, c, :]) for c in range(2)], *u_.free)
                t_h = dve.do([t, t_g], nc.vector.tensor_tensor, s_.t[0:m, 1, :], u_.t[0:m, :], s_.t[0:m, 0, :], ALU.mult)
                u_.done(t_h)

                def down():
                    pe.wait(t_h, arrived(oname))
                    for i in range(NT):
                        t = add(i, s_.t[0:m, 1, i * P:(i + 1) * P], w(oname)[0:m, n, :], (0, D))
                    s_.done(t)
                return down

            late = []
            for n in range(8):
                late.append(swiglu("wsg", "wout", n, P, 1024, 0, y.t, t_y))
                if len(late) > 1:
                    late.pop(0)()
            y.done((pe.sem, pe.n))
            for n in range(4):
                late.append(swiglu("sgu", "sdn", n, 88, 0, 352, xn.t, t_xn))
                late.pop(0)()
            late.pop(0)()
            yield

            for n in range(E):
                k, turn = ms["n"] % 2, ms["n"] // 2 + 1
                ms["n"] += 1
                t_mg = sp.dma(mg[k][:, :, :], gu[n], s_mg[k], turn, *ms["free"][k])
                t_md = sp.dma(md[k][:, :, :], dn[n], s_md[k], turn)

                def expert(i):
                    g_ = banks.take()
                    t = product(g_.t[:, 0:352], [(xn.t[:, c, i * P:(i + 1) * P], mg[k][:, c, :]) for c in range(2)], t_mg, t_xn, *g_.free)
                    t = act.do([t, sgfree[i]], nc.scalar.activation, sg[i][:, :], g_.t[:, 0:176], ACT.Silu)
                    t = dve.do([t, t_comb, hfree[i]], nc.vector.scalar_tensor_tensor, hh[i][:, :], sg[i][:, :], comb[:, i, n:n + 1], g_.t[:, 176:352], ALU.mult, ALU.mult)
                    sgfree[i] = t
                    g_.done(t)
                    return t

                def expert_down(i, t):
                    b_ = banks.take()
                    pe.wait(t, *b_.free)
                    for c in range(2):
                        t = pe.do([], nc.tensor.transpose, b_.t[0:88, c * P:(c + 1) * P], hh[i][:, c * 88:(c + 1) * 88], ident)
                    hfree[i] = t
                    t = act.do([t, tfree[i]], nc.scalar.activation, hT[i][:, :, :], b_.t[0:88, 0:2 * P].rearrange("p (c t) -> p c t", c=2), ACT.Copy)
                    b_.done(t)
                    return t

                def expert_add(i, t):
                    pe.wait(t, t_md)
                    for c in range(2):
                        t = add(i, hT[i][:, c, :], md[k][:, c, :], (0, D))
                    tfree[i] = t
                    return t

                ts = [expert(i) for i in range(NT)]
                ts = [expert_down(i, t) for i, t in enumerate(ts)]
                for i, t in enumerate(ts):
                    t = expert_add(i, t)
                ms["free"][k] = [t]
            xn.done(t)
            o = ob[b % 2]
            for i in range(2):
                t_o = dve.do([t, out_done.get(b - 2)], nc.vector.tensor_copy, o[:, 2 * i:2 * i + 2, :], acc[i].t[:, :].rearrange("p (i d) -> p i d", i=2))
                acc[i].done(t_o)
            out_done[b] = sp.dma(out[b].rearrange("(i p) d -> p i d", p=P), o[:, :, :], s_out[b % 2], b // 2 + 1, t_o)
            yield

        sgfree, hfree, tfree = [None] * NT, [None] * NT, [None] * NT
        for b in range(NB):
            for _ in layer0(b):
                pass
            for _ in layer1(b):
                pass
        sp.wait(out_done[NB - 2], out_done[NB - 1])

        block = ctx.enter_context(nc.Block())

        @block.sync
        def _(e):
            sp.play(e)

        @block.tensor
        def _(e):
            pe.play(e)

        @block.scalar
        def _(e):
            act.play(e)

        @block.vector
        def _(e):
            dve.play(e)

        @block.gpsimd
        def _(e):
            pool.play(e)


def rows(a, n=P):
    return a.reshape(-1, n, a.shape[-1]).transpose(1, 0, 2)


def kernel(**inputs):
    import numpy as _np
    import concourse.bacc as _bacc
    from concourse import mybir as _mybir
    from concourse.bass_utils import run_bass_kernel_spmd as _run

    a = {k: _np.asarray(v) for k, v in inputs.items()}

    def cols(v):
        return v.reshape(-1, P).T

    cst = _np.zeros((P, 8 + 2 * P + 16), _np.float32)
    cst[:, C_LN] = LN_EPS
    cst[:, C_LNR] = LN_EPS * EPS
    cst[:, C_RMS] = EPS
    cst[:, 8:8 + P] = _np.eye(P)
    cst[:, 8 + P:8 + 2 * P] = 1.0 / D
    cst[:, 8 + 2 * P:] = _np.arange(16)
    genes = _np.concatenate([a["L0_ffn_genes"], _np.ones((512, 32), _np.float32)], 1)
    arrays = {
        "x": a["L0_attn_x"].transpose(0, 2, 1).reshape(NB, 2, P, T).transpose(0, 2, 1, 3),
        "vec": _np.concatenate([
            cols(a["L0_attn_bq"]), cols(a["L0_attn_bk"]), cols(a["L0_attn_bv"]), cols(a["L0_attn_bo"]), cols(a["L0_ffn_norm_w"]),
            _np.broadcast_to(a["L0_ffn_scale"], (P, 1)), _np.broadcast_to(a["L0_ffn_temperature"], (P, 1))], 1),
        "cst": cst,
        "wqkv0": rows(_np.concatenate([a["L0_attn_Wq"].T, a["L0_attn_Wk"].T, a["L0_attn_Wv"].T], 1)),
        "wo0": rows(a["L0_attn_Wo"].T),
        "wc": rows(a["L0_ffn_Wc"].T),
        "genes": rows(genes),
        "wdu": _np.concatenate([a["L0_ffn_Wd"].T, a["L0_ffn_Wu"].T], 1),
        "wqkv1": rows(a["L1_attn_w_qkv"].T),
        "wsg": rows(a["L1_attn_w_swiglu"].T),
        "wout": rows(a["L1_attn_w_out"].T),
        "gate": rows(a["L1_ffn_gate_w"].T),
        "sgu": rows(a["L1_ffn_shared_gate_up"]),
        "sdn": rows(a["L1_ffn_shared_down"], 88),
        "gu": a["L1_ffn_w_gate_up"].reshape(E, 2, P, 352).transpose(0, 2, 1, 3),
        "dn": a["L1_ffn_w_down"].reshape(E, 2, 88, D).transpose(0, 2, 1, 3),
    }
    nc = _bacc.Bacc("TRN2", target_bir_lowering=False, num_devices=1)
    sent, aps = {}, {}
    for k, v in arrays.items():
        v = _np.ascontiguousarray(v)
        sent["in_" + k] = v
        aps[k] = nc.dram_tensor("in_" + k, v.shape, _mybir.dt.from_np(v.dtype), kind="ExternalInput").ap()
    aps["out"] = nc.dram_tensor("out_0", (NB, T, D), _mybir.dt.float32, kind="ExternalOutput").ap()
    build(nc, **aps)
    r = _run(nc, [sent], core_ids=[0])
    return r.results[0]["out_0"]
```

```python
from contextlib import ExitStack

import numpy as np

import concourse.bass as bass
from concourse import mybir

F32 = mybir.dt.float32
F32R = mybir.dt.float32r
U32 = mybir.dt.uint32
ALU = mybir.AluOpType
ACT = mybir.ActivationFunctionType
AX = mybir.AxisListType.X

P = 128
NB = 4
T = 512
D = 256
NT = T // P
E = 16
EPS = 2.0 ** -23
LN_EPS = 1e-5
LOWEST = -3.4e38

TILES = 47
TW = 48
EW = 2 * 352 + 2 * D

V_BQ, V_BK, V_BV, V_BO, V_NW, V_SC, V_TP = 0, 2, 4, 6, 8, 10, 11
C_LN, C_LNR, C_RMS = 0, 1, 2
C_ID, C_MEAN, C_TRI, C_IOTA, C_TOK, CW = 8, 136, 264, 392, 520, 536


class Queue:

    def __init__(self, sem):
        self.sem, self.n, self.ops, self.seen = sem, 0, [], {}

    def wait(self, *tokens):
        for t in tokens:
            if t is None:
                continue
            sem, value = t
            if self.seen.get(id(sem), 0) < value:
                self.seen[id(sem)] = value
                self.ops.append(lambda e, s=sem, v=value: e.wait_ge(s, v))

    def do(self, waits, fn, *args, **named):
        self.wait(*waits)
        self.n += 1
        self.ops.append(lambda e: fn(*args, **named).then_inc(self.sem, 1))
        return (self.sem, self.n)

    def run(self, waits, fn, *args, **named):
        self.wait(*waits)
        self.ops.append(lambda e: fn(*args, **named))

    def dma(self, waits, out, in_, sem, count):
        self.wait(*waits)
        self.ops.append(lambda e: e.dma_start(out, in_).then_inc(sem, 16))
        return (sem, 16 * count)

    def now(self):
        return (self.sem, self.n)

    def play(self, e):
        for op in self.ops:
            op(e)


class Place:

    def __init__(self, t, r=None, sem=None):
        self.t, self.r, self.sem, self.turns, self.free, self.held = t, r, sem, 0, [], False

    def done(self, *tokens):
        assert self.held
        self.free, self.held = list(tokens), False


class Ring:
    def __init__(self, places):
        self.order = list(places)

    def take(self):
        for i, p in enumerate(self.order):
            if not p.held:
                self.order.append(self.order.pop(i))
                p.held = True
                return p
        return None


def take(*rings):
    for r in rings:
        p = r.take()
        if p:
            return p
    raise AssertionError("every place is held")


def build(nc, x, vec, cst, wqkv0, wo0, wc, genes, wdu, wqkv1, wsg, wout, gate, sgu, sdn, gu, dn, part_d, out):
    with ExitStack() as ctx:
        base = nc.sbuf_base + (-nc.sbuf_base) % 32
        arena = ctx.enter_context(nc.sbuf_tensor("arena", [P, 53180], F32))
        at = [0]

        def put(name, words, dt=F32, parts=P):
            t = nc.alloc_sbuf_tensor_at(name, [parts, words], dt, offset=base + 4 * at[0])
            at[0] += words + (-words) % 8
            assert at[0] <= 53180, at
            return t

        def sem(name):
            return ctx.enter_context(nc.semaphore(name))

        pe, act, dve, pool, sp = (Queue(sem(f"s_{n}")) for n in ("pe", "act", "dve", "pool", "sp"))
        V, A, G, M = nc.vector, nc.scalar, nc.gpsimd, nc.tensor

        bank_ring = Ring([Place(ctx.enter_context(nc.psum_tensor(f"bank{i}", [P, 512], F32))) for i in range(8)])

        def bank():
            return take(bank_ring)

        W = {}

        def weight(name, ap, words, parts=P):
            W[name] = (put("w_" + name, words, parts=parts), sem("d_" + name), ap)

        def slot(name):
            o = at[0]
            f = put(name, 1024)
            r = nc.alloc_sbuf_tensor_at(name + "r", [P, 1024], F32R, offset=base + 4 * o)
            return Place(f[:, :].rearrange("p (c t) -> p c t", c=2), r[:, :].rearrange("p (c t) -> p c t", c=2))

        for name, ap, words in (("wqkv0", wqkv0, 1536), ("wc", wc, 1024), ("wo0", wo0, 512), ("genes", genes, 384)):
            weight(name, ap, words)
        weight("wdu", wdu, 512, 96)
        wdu_r = put("wdu_r", 512, F32R, 96)
        weight("wqkv1", wqkv1, 1536)
        front_slots = Ring([slot(f"sf{i}") for i in range(8)])
        assert at[0] <= 12 * EW
        at[0] = 12 * EW
        late_slots = Ring([slot(f"sl{i}") for i in range(4)])
        at[0] = E * EW
        mw = nc.alloc_sbuf_tensor_at("mw", [P, E * EW], F32, offset=base)
        s_mw = [sem(f"d_mw{i}") for i in range(8)]
        slots = Ring([slot(f"sg{i}") for i in range(4)])
        h_slots = Ring([slot(f"sh{i}") for i in range(4)])
        weight("cst", cst, CW)
        weight("vec", vec, 12)
        weight("gate", gate, 2 * E)
        pairs = {n: (put(n + "_h", k, F32R), put(n + "_l", k, F32R)) for n, k in (("wsg", 4096), ("wout", 2048), ("sgu", 1408), ("sdn", 768))}
        res = put("rows", 16 * D)
        rows_ = res[:, :].rearrange("p (i d) -> p i d", d=D)
        misc = put("misc", 64)
        m8s = [put(f"m8{i}", 32) for i in range(2)]
        nbs = [put(f"nb{i}", 8) for i in range(2)]
        g_m = put("g_m", 4)
        g_s = put("g_s", 64)
        g_8 = put("g_8", 32)
        g_i = put("g_i", 32, U32)
        g_f = put("g_f", 8)
        hot = put("hot", 2 * 256)
        gval = put("gval", 32)
        slot_i = put("slot_i", 32, U32)
        slot_q = put("slot_q", 64, U32)
        slot_f = put("slot_f", 64)
        tab = put("tab", TW, U32)
        eoff = put("eoff", TW, U32)
        e_n = put("e_n", 96)
        e_u = put("e_u", 32, U32)

        def cells(name, n, words, parts=P):
            return Ring([Place(put(f"{name}{i}", words, parts=parts)) for i in range(n)])

        def dma_cells(name, n, words):
            r = cells(name, n, words)
            for i, p in enumerate(r.order):
                p.sem = sem(f"d_{name}{i}")
            return r

        xg = dma_cells("xg", 3, D)
        m_xt = cells("m_xt", 2, D)
        m_h = cells("m_h", 3, 176)
        m_ht = cells("m_ht", 2, D, 88)
        m_y = dma_cells("m_y", 2, D)
        s_x = [sem(f"d_x{i}") for i in range(NB)]
        s_xn = [sem(f"d_xn{i}") for i in range(NB)]
        s_st = [sem(f"d_st{i}") for i in range(9)]
        s_out = [sem(f"d_out{i}") for i in range(NB)]
        s_part = sem("d_part")
        s_ga = [sem(f"d_ga{i}") for i in range(32)]

        xn_d = nc.dram_tensor("xn_rows", (NB * T, D), F32).ap()
        y_d = nc.dram_tensor("y_rows", (TILES * P, D), F32).ap()

        c_t = W["cst"][0]
        ident = c_t[:, C_ID:C_ID + P]
        mean = c_t[:, C_MEAN:C_MEAN + P]
        tri = c_t[:, C_TRI:C_TRI + P]
        iota = c_t[:, C_IOTA:C_IOTA + P]
        tokid = c_t[:, C_TOK:C_TOK + 16]

        def w(name, inner=None):
            t = W[name][0][:, :]
            return t if inner is None else t.rearrange("p (c n) -> p c n", n=inner)

        def pair(name, inner):
            return [t[:, :].rearrange("p (c n) -> p c n", n=inner) for t in pairs[name]]

        def arrived(name):
            return (W[name][1], 16)

        def col(i):
            return w("vec")[:, i:i + 1]

        def con(i):
            return c_t[:, i:i + 1]

        def load(name):
            t, s, ap = W[name]
            sp.dma([], t[:, :], ap, s, 1)

        def product(out_, terms, *waits):
            pe.wait(*waits)
            for i, (a, b) in enumerate(terms):
                first, last = i == 0, i == len(terms) - 1
                if last:
                    return pe.do([], M.matmul, out_, a, b, start=first, stop=last)
                pe.run([], M.matmul, out_, a, b, start=first, stop=last)

        def three(ah, al, bh, bl):
            return [(ah, bh), (al, bh), (ah, bl)]

        def wide(ap):
            return ap[:, None, :].broadcast_to([P, 2, T])

        def split(src, t, *rings):
            h, l = take(*rings), take(*rings)
            for c in range(2):
                t1 = act.do([t, *h.free], A.activation, h.r[:, c, :], src[:, c, :], ACT.Copy)
                t2 = pool.do([t1, *l.free], G.tensor_tensor, l.r[:, c, :], src[:, c, :], h.r[:, c, :].bitcast(F32), ALU.subtract)
            return h, l, t2

        FR = [front_slots, late_slots, slots, h_slots]

        def norm(src, t_src, fold):
            m = bank()
            sq = take(*FR)
            if fold:
                t = pool.do([*t_src, *sq.free], G.tensor_tensor, sq.t[:, 0, :], src[:, 0, :], src[:, 1, :], ALU.add)
                t = product(m.t[:, :], [(mean, sq.t[:, 0, :])], t, *m.free)
            else:
                t = product(m.t[:, :], [(mean, src[:, c, :]) for c in range(2)], *t_src, *m.free)
            xc = take(*FR)
            t_xc = dve.do([t, *xc.free], V.tensor_tensor, xc.t, src, wide(m.t[:, :]), ALU.subtract)
            m.done(t_xc)
            yield
            t = act.do([t_xc, t, *sq.free], A.activation, sq.t, xc.t, ACT.Square)
            v = bank()
            if fold:
                t = pool.do([t], G.tensor_tensor, sq.t[:, 0, :], sq.t[:, 0, :], sq.t[:, 1, :], ALU.add)
                t = product(v.t[:, :], [(mean, sq.t[:, 0, :])], t, *v.free)
            else:
                t = product(v.t[:, :], [(mean, sq.t[:, c, :]) for c in range(2)], t, *v.free)
            sq.done(t)
            yield
            r = take(*FR)
            act.do([t, *r.free], A.activation, r.t[:, 0, :], v.t[:, :], ACT.Ln, bias=con(C_LN))
            t = act.do([], A.activation, r.t[:, 1, :], v.t[:, :], ACT.Ln, bias=con(C_LNR), scale=1.0 + EPS)
            v.done(t)
            t_r = act.do([t], A.activation, r.t, r.t, ACT.Exp, scale=-0.5)
            return xc, t_xc, r, t_r

        def scan(dst, src, init, *waits):
            for c in range(2):
                t = dve.do(waits, V.tensor_tensor_scan, dst[:, c, :], src[:, c, :], src[:, c, :], init, ALU.add, ALU.bypass)
            return t

        xsl, xtok = {}, {}

        def fetch(b):
            s = take(*FR)
            xsl[b] = s
            xtok[b] = sp.dma(s.free, s.t, x[b], s_x[b], 1)

        def half(g):
            for y in g:
                if y == "middle":
                    return
                yield

        def merge(*streams):
            live = [[g, n] for g, n in streams]
            while live:
                for s in list(live):
                    for _ in range(s[1]):
                        if next(s[0], "end") == "end":
                            live.remove(s)
                            break

        em_free, top_last, scaled = [None, None], [None, None], [None, None]
        t_mgate = [None]
        state = {}

        def front(b, fold=True):
            src, t_src = xsl[b], xtok[b]
            m8, nb = m8s[b % 2], nbs[b % 2]
            xc, t_xc, r, t_r = yield from norm(src.t, [t_src, arrived("cst")], fold)
            xn, xnn = take(*FR), take(*FR)
            t_xn = dve.do([t_r, *xn.free], V.tensor_tensor, xn.t, xc.t, wide(r.t[:, 0, :]), ALU.mult)
            for c in range(2):
                t_xnn = dve.do([arrived("vec"), *xnn.free], V.scalar_tensor_tensor, xnn.t[:, c, :], xc.t[:, c, :], col(V_NW + c), r.t[:, 1, :], ALU.mult, ALU.mult)
            xc.done(t_xnn)
            r.done(t_xnn)
            yield

            ets = [take(*FR), take(*FR)]
            last = {}

            def top(i):
                b_ = bank()
                t = product(b_.t[:, :], [(xnn.t[:, c, i * P:(i + 1) * P], w("wc", 512)[:, c, :]) for c in range(2)], arrived("wc"), t_xnn, *b_.free)
                wk = take(*FR)
                wt, em = wk.t[:, 0, :], wk.t[:, 1, :]
                t = dve.do([t, top_last[b % 2]], V.max, m8[:, 0:8], b_.t[:, :])
                t1 = dve.do([t, t_it, em_free[b % 2]], V.tensor_scalar, nb[:, 0:1], m8[:, 0:1], nit, None, ALU.mult)
                t = dve.do([*wk.free], V.match_replace, wt, m8[:, 0:8], b_.t[:, :], LOWEST)
                t_e = act.do([t1, t], A.activation, em, b_.t[:, :], ACT.Exp, bias=nb[:, 0:1], scale=it)
                em_free[b % 2] = t_e
                b_.done(t_e)
                yield
                for k in range(1, 4):
                    t = dve.do([t], V.max, m8[:, 8 * k:8 * k + 8], wt)
                    t = dve.do([t], V.match_replace, wt, m8[:, 8 * k:8 * k + 8], wt, LOWEST)
                t = dve.do([t, t_e], V.scalar_tensor_tensor, em, wt, LOWEST / 1.1, em, ALU.is_le, ALU.mult, accum_out=nb[:, 1:2])
                top_last[b % 2] = t
                t = dve.do([t, scaled[b % 2]], V.reciprocal, nb[:, 2:3], nb[:, 1:2])
                t = pool.do([t], G.tensor_scalar, em, em, nb[:, 2:3], 1.0, ALU.mult, ALU.mult)
                scaled[b % 2] = t
                yield
                b_ = bank()
                pe.wait(t, *b_.free)
                for g in range(4):
                    t = pe.do([], M.transpose, b_.t[:, g * P:(g + 1) * P], em[:, g * P:(g + 1) * P], ident)
                wk.done(t)
                for h in range(2):
                    last["et"] = act.do([t, *ets[h].free], A.activation, ets[h].t[:, :, i * P:(i + 1) * P],
                                        b_.t[:, h * 2 * P:(h + 1) * 2 * P].rearrange("p (g t) -> p g t", g=2), ACT.Copy)
                b_.done(last["et"])
                yield

            def project(j):
                b_ = bank()
                t = product(b_.t[:, :], [(w("wqkv0", 768)[:, c, j * P:(j + 1) * P], xn.t[:, c, :]) for c in range(2)],
                            arrived("wqkv0"), t_xn, *b_.free)
                return b_, t

            def phi(j0, bias):
                ph, rl = take(*FR), take(*FR)
                for j in range(2):
                    b_, t = project(j0 + j)
                    act.do([t, arrived("vec"), *ph.free], A.activation, ph.t[:, j, :], b_.t[:, :], ACT.Exp, bias=col(bias + j))
                    t = act.do([*rl.free], A.activation, rl.t[:, j, :], b_.t[:, :], ACT.Relu, bias=col(bias + j))
                    b_.done(t)
                    yield
                t = dve.do([t], V.scalar_tensor_tensor, ph.t, ph.t, 1.0, rl.t, ALU.min, ALU.add)
                rl.done(t)
                return ph, t

            def attend():
                phk, t_phk = yield from phi(2, V_BK)
                pv = take(*FR)
                for j in range(2):
                    b_, t = project(4 + j)
                    t_pv = dve.do([t, t_phk, *pv.free], V.scalar_tensor_tensor, pv.t[:, j, :], b_.t[:, :], col(V_BV + j), phk.t[:, j, :], ALU.add, ALU.mult)
                    b_.done(t_pv)
                    yield
                phk.done(t_pv)
                kv = take(*FR)
                t_kv = scan(kv.t, pv.t, 0.0, t_pv, *kv.free)
                pv.done(t_kv)
                phq, t_phq = yield from phi(0, V_BQ)
                xn.done(pe.now())
                t = dve.do([t_phq, t_kv], V.scalar_tensor_tensor, kv.t, phq.t, 0.25, kv.t, ALU.mult, ALU.mult)
                phq.done(t)
                last["ctx"] = (kv, t)
                yield

            def tops():
                for i in range(NT):
                    yield from top(i)

            streams = [attend(), tops()]
            while streams:
                for s in list(streams):
                    if next(s, "end") == "end":
                        streams.remove(s)
                    else:
                        yield
            kv, t_ctx = last["ctx"]
            t_et = last["et"]

            b_ = bank()
            t = product(b_.t[0:96, :], [(w("genes", 96)[:, g, :], ets[g // 2].t[:, g % 2, :]) for g in range(4)], arrived("genes"), t_et, *b_.free)
            for s in ets:
                s.done(t)
            x_ = take(*FR)
            xr_ = x_.r[0:96, 0, :]
            t = act.do([t, *x_.free], A.activation, xr_, b_.t[0:96, :], ACT.Copy)
            t_ex = dve.do([t], V.tensor_tensor, x_.r[64:96, 0, :], b_.t[64:96, :], x_.r[64:96, 0, :].bitcast(F32), ALU.subtract)
            b_.done(t_ex)
            yield
            th, up = take(*FR), take(*FR)
            for j in range(2):
                d_, u_ = bank(), bank()
                t = product(d_.t[:, :], [(wdu_r[:, j * P:(j + 1) * P], xr_)], t_wdu[0], t_ex, *d_.free)
                t_t = act.do([t, *th.free], A.activation, th.t[:, j, :], d_.t[:, :], ACT.Tanh)
                d_.done(t_t)
                t = product(u_.t[:, :], [(wdu_r[:, D + j * P:D + (j + 1) * P], xr_)], *u_.free)
                t_up = dve.do([t, t_t, *up.free], V.scalar_tensor_tensor, up.t[:, j, :], u_.t[:, :], col(V_SC), th.t[:, j, :], ALU.mult, ALU.mult)
                u_.done(t_up)
                yield
            x_.done(t)
            th.done(t_up)
            t_up = pool.do([t_up], G.tensor_tensor, up.t, up.t, xnn.t, ALU.mult)
            xnn.done(t_up)
            x1 = take(*FR)
            t_up = pool.do([t_up], G.tensor_tensor, up.t, up.t, src.t, ALU.add)
            src.done(t_up)
            for j in range(2):
                b_ = bank()
                t = product(b_.t[:, :], [(w("wo0", D)[:, c, j * P:(j + 1) * P], kv.t[:, c, :]) for c in range(2)], arrived("wo0"), t_ctx, *b_.free)
                t_x1 = dve.do([t, t_up, *x1.free], V.scalar_tensor_tensor, x1.t[:, j, :], b_.t[:, :], col(V_BO + j), up.t[:, j, :], ALU.add, ALU.add)
                b_.done(t_x1)
            kv.done(t)
            up.done(t_x1)
            yield "middle"

            xc, t_xc, r, t_r = yield from norm(x1.t, [t_x1], fold)
            xn2, xr = take(*FR), take(*FR)
            t_xr = dve.do([t_r, *xr.free], V.tensor_tensor, xr.t, xc.t, wide(r.t[:, 1, :]), ALU.mult)
            t_xn2 = dve.do([*xn2.free], V.tensor_tensor, xn2.t, xc.t, wide(r.t[:, 0, :]), ALU.mult)
            xc.done(t_xn2)
            r.done(t_xn2)
            t_s = pool.do([t_xn2], G.tensor_tensor, x1.t, x1.t, xn2.t, ALU.add)
            yield
            raw = []
            for j in range(2):
                b_ = bank()
                t = product(b_.t[:, :], [(w("wqkv1", 768)[:, c, j * P:(j + 1) * P], xr.t[:, c, :]) for c in range(2)], arrived("wqkv1"), t_xr, *b_.free)
                raw.append((b_, t))
            yield
            homes = [(late_slots, slots), (slots, late_slots)][b % 2][:1 + (b < 2)]

            def turned():
                t_w = []
                for srct, t0, dst in ((xn2, t_xn2, None), (x1, t_s, rows_)):
                    o = take(*FR) if dst is None else None
                    for h in range(2):
                        b_ = bank()
                        pe.wait(t0, *b_.free)
                        for n in range(4):
                            i, c = 2 * h + n // 2, n % 2
                            t = pe.do([], M.transpose, b_.t[:, n * P:(n + 1) * P], srct.t[:, c, i * P:(i + 1) * P], ident)
                        if o:
                            t1 = act.do([t, *o.free], A.activation, o.t[:, h, :], b_.t[:, :], ACT.Copy)
                        else:
                            t1 = act.do([t], A.activation, dst[:, 4 * b + 2 * h:4 * b + 2 * h + 2, :], b_.t[:, :].rearrange("p (i d) -> p i d", d=D), ACT.Copy)
                        b_.done(t1)
                        yield
                    if o:
                        t2 = sp.dma([t1], xn_d[b * T:(b + 1) * T, :].rearrange("(i p) d -> p i d", p=P), o.t.rearrange("p h (i d) -> p (h i) d", d=D), s_xn[b], 1)
                        o.done(t2)
                        t_w.append(t2)
                    else:
                        x1.done(t)
                        state["rows", b] = t1
                state["xn", b] = t_w[0]

            def gates():
                b_ = bank()
                pe.wait(arrived("gate"), t_xn2, *b_.free)
                for i in range(NT):
                    t = product(b_.t[:, i * E:(i + 1) * E], [(xn2.t[:, c, i * P:(i + 1) * P], w("gate", E)[:, c, :]) for c in range(2)])

                def v3(tt, n=E):
                    return tt.rearrange("p (i e) -> p i e", e=n)

                gl, gs, g8 = v3(b_.t[:, 0:NT * E]), v3(g_s[:, :]), v3(g_8[:, :], 8)
                gm = g_m[:, 0:4, None].broadcast_to([P, NT, E])
                t = dve.do([t], V.tensor_reduce, g_m[:, 0:4], gl, AX, ALU.max)
                t = dve.do([t], V.tensor_tensor, gs, gl, gm, ALU.subtract)
                b_.done(t)
                t = act.do([t], A.activation, gs, gs, ACT.Exp)
                yield
                t = dve.do([t], V.tensor_reduce, g_m[:, 0:4], gs, AX, ALU.add)
                t = dve.do([t], V.reciprocal, g_m[:, 0:4], g_m[:, 0:4])
                t = dve.do([t], V.tensor_tensor, gs, gs, gm, ALU.mult)
                for i in range(NT):
                    t1 = dve.do([t], V.max, g8[:, i, :], gs[:, i, :])
                for i in range(NT):
                    t = dve.do([t1], V.max_index, v3(g_i[:, :], 8)[:, i, :], g8[:, i, :], gs[:, i, :])
                gv = v3(gval[:, :], 2)[:, 4 * b:4 * b + 4, :]
                dve.do([], V.tensor_copy, gv, g8[:, :, 0:2])
                t = dve.do([t], V.tensor_copy, v3(g_f[:, :], 2), v3(g_i[:, :], 8)[:, :, 0:2])
                for k in range(2):
                    ho = v3(hot[:, k * 256 + 64 * b:k * 256 + 64 * b + 64])
                    t1 = dve.do([t], V.tensor_tensor, ho, iota[:, None, 0:E].broadcast_to([P, NT, E]),
                                v3(g_f[:, :], 2)[:, :, k:k + 1].broadcast_to([P, NT, E]), ALU.is_equal)
                state["hot", b] = t1
                yield

            t_y2 = {}

            def ykv():
                hat = []
                for n in range(2):
                    if n:
                        for j in range(2, 4):
                            b_ = bank()
                            t = product(b_.t[:, :], [(w("wqkv1", 768)[:, c, j * P:(j + 1) * P], xr.t[:, c, :]) for c in range(2)], *b_.free)
                            raw.append((b_, t))
                    sq = take(*FR)
                    for j in range(2):
                        b_, t = raw[2 * n + j]
                        t_sq = act.do([t, *sq.free], A.activation, sq.t[:, j, :], b_.t[:, :], ACT.Square)
                    yield
                    m = bank()
                    if fold:
                        t = pool.do([t_sq], G.tensor_tensor, sq.t[:, 0, :], sq.t[:, 0, :], sq.t[:, 1, :], ALU.add)
                        t = product(m.t[:, :], [(mean, sq.t[:, 0, :])], t, *m.free)
                    else:
                        t = product(m.t[:, :], [(mean, sq.t[:, c, :]) for c in range(2)], t_sq, *m.free)
                    t = act.do([t], A.activation, sq.t[:, 0, :], m.t[:, :], ACT.Ln, bias=con(C_RMS))
                    m.done(t)
                    t = act.do([t], A.activation, sq.t[:, 0, :], sq.t[:, 0, :], ACT.Exp, scale=-0.5)
                    h = take(*FR)
                    for j in range(2):
                        b_ = raw[2 * n + j][0]
                        t1 = dve.do([t, *h.free], V.tensor_tensor, h.t[:, j, :], b_.t[:, :], sq.t[:, 0, :], ALU.mult)
                        b_.done(t1)
                    sq.done(t1)
                    t1 = act.do([t1], A.activation, h.t, h.t, ACT.Exp, scale=(-1.0, 1.0)[n])
                    hat.append((h, t1))
                    yield
                (eq, t_eq), (wk, t_wk) = hat
                wv = take(*FR)
                for j in range(2):
                    b_ = bank()
                    t = product(b_.t[:, :], [(w("wqkv1", 768)[:, c, (4 + j) * P:(5 + j) * P], xr.t[:, c, :]) for c in range(2)], *b_.free)
                    t_wv = dve.do([t, t_wk, *wv.free], V.tensor_tensor, wv.t[:, j, :], b_.t[:, :], wk.t[:, j, :], ALU.mult)
                    b_.done(t_wv)
                    yield
                xr.done(t)
                kc, wc_ = take(*FR), take(*FR)
                t_kc = scan(kc.t, wv.t, 0.0, t_wv, *kc.free)
                t_wc = scan(wc_.t, wk.t, 1e-6, *wc_.free)
                wv.done(t_kc)
                wk.done(t_wc)
                yield
                t = dve.do([t_eq, t_wc], V.scalar_tensor_tensor, eq.t, eq.t, 1.0, wc_.t, ALU.add, ALU.mult)
                for c in range(2):
                    t = dve.do([t], V.reciprocal, eq.t[:, c, :], eq.t[:, c, :])
                    t_y = dve.do([t], V.tensor_tensor, kc.t[:, c, :], kc.t[:, c, :], eq.t[:, c, :], ALU.mult)
                    yield
                wc_.done(t_y)
                eq.done(t_y)
                yh, yl, t = split(kc.t, t_y, *homes)
                kc.done(t)
                state["y", b] = (yh, yl, t)
                yield

            streams = [ykv(), gates(), turned()]
            while streams:
                for s in list(streams):
                    if next(s, "end") == "end":
                        streams.remove(s)
                    else:
                        yield
            xh, xl, t = split(xn2.t, t_xn2, *homes)
            xn2.done(t, pe.now(), act.now())
            state["x2", b] = (xh, xl, t)
            yield

        HS = {}
        RT = (slots, late_slots, h_slots)

        def dense(b, direct, parts=(0, 1)):
            yh, yl, t_y = state["y", b]
            xh, xl, t_x = state["x2", b]
            if 0 in parts:
                state["acc", b] = [bank(), bank()]
                for a in state["acc", b]:
                    pe.wait(*a.free)
            acc = state["acc", b]
            H = (h_slots,)

            def chunk(k):
                if k < 8:
                    wn, on, inner, m, n, go, uo, sh, sl, t_s = "wsg", "wout", 2048, P, k, 1024, 0, yh, yl, t_y
                else:
                    wn, on, inner, n, go, uo, sh, sl, t_s = "sgu", "sdn", 704, k - 8, 0, 352, xh, xl, t_x
                    m = min(P, 352 - n * P)
                wh, wl = pair(wn, inner)
                oh, ol = pair(on, D)
                ps = []
                s_ = take(*H)

                def gather(o):
                    b_ = bank()
                    terms = []
                    for c in range(2):
                        a, al = (z[:, c, o + n * P:o + n * P + m] for z in (wh, wl))
                        terms += three(a, al, sh.r[:, c, :], sl.r[:, c, :])
                    terms.sort(key=lambda z: z[1] is None)
                    return b_, product(b_.t[0:m, :], terms, prepared[wn], t_s, *b_.free)

                g_, t = gather(go)
                if direct:
                    t_g = act.do([t, *s_.free], A.activation, s_.t[0:m, 0, :], g_.t[0:m, :], ACT.Silu)
                else:
                    t_g = act.do([t, *s_.free], A.activation, s_.t[0:m, 0, :], g_.t[0:m, :], ACT.Tanh, scale=0.5)
                    t_g = dve.do([t_g], V.scalar_tensor_tensor, s_.t[0:m, 0, :], s_.t[0:m, 0, :], 1.0, g_.t[0:m, :], ALU.add, ALU.mult)
                g_.done(t_g)
                u_, t = gather(uo)
                t_h = dve.do([t, t_g], V.scalar_tensor_tensor, s_.t[0:m, 1, :], s_.t[0:m, 0, :], 1.0 if direct else 0.5, u_.t[0:m, :], ALU.mult, ALU.mult)
                u_.done(t_h)
                r_ = take(*H)
                t1 = act.do([t_h, *r_.free], A.activation, r_.r[0:m, 0, :], s_.t[0:m, 1, :], ACT.Copy)
                t2 = pool.do([t1], G.tensor_tensor, r_.r[0:m, 1, :], s_.t[0:m, 1, :], r_.r[0:m, 0, :].bitcast(F32), ALU.subtract)
                s_.done(t1, t2)

                def down():
                    pe.wait(t2, prepared[on])
                    for i in range(NT):
                        a = acc[i // 2].t[:, (i % 2) * D:(i % 2 + 1) * D]
                        h0, h1 = (r_.r[0:m, z, i * P:(i + 1) * P] for z in range(2))
                        for z, (p, q) in enumerate(((h0, oh), (h0, ol), (h1, oh))):
                            f = k == 0 and i % 2 == 0 and z == 0
                            t = pe.do([], M.matmul, a, p, q[0:m, n, :], start=f, stop=False, skip_group_check=True)
                    r_.done(t)
                return down

            late = HS.setdefault(b, [])
            for k in (range(8) if 0 in parts else []):
                late.append(chunk(k))
                if len(late) > 1:
                    late.pop(0)()
                yield
            if 0 in parts:
                yh.done(pe.now())
                yl.done(pe.now())
            if 1 in parts:
                for k in range(8, 11):
                    late.append(chunk(k))
                    late.pop(0)()
                    yield
                late.pop(0)()
                xh.done(pe.now())
                xl.done(pe.now())
                for i in range(2):
                    o = rows_[:, 4 * b + 2 * i:4 * b + 2 * i + 2, :]
                    t = dve.do([pe.now(), state["rows", b]], V.tensor_tensor, o, acc[i].t[:, :].rearrange("p (i d) -> p i d", d=D), o, ALU.add)
                    acc[i].done(t)
                state["rows", b] = t
                yield

        def route():
            t_hot = [state["hot", b] for b in range(NB)]
            s0, s1, s2 = take(*RT), take(*RT), take(*RT)
            hk = [hot[:, k * 256:(k + 1) * 256] for k in range(2)]
            mm = s0.t[:, 0, 0:256]
            t = dve.do([*t_hot, *s0.free], V.tensor_tensor, mm, hk[0], hk[1], ALU.add)
            b_ = bank()
            product(b_.t[:, 0:256], [(tri, mm)], t, *b_.free)
            t = product(b_.t[:, 256:512], [(mean, mm)])

            def ei(ap):
                return ap.rearrange("p (i e) -> p e i", e=E)

            cnt, inc, bas, pos = s0.t[:, 0, 256:512], s0.t[:, 1, 0:256], s0.t[:, 1, 256:512], s1.t[:, 0, 0:256]
            part = s1.t[:, 0, 256:512]
            t_part = sp.dma(s1.free, part, part_d, s_part, 1)

            def g3(ap):
                return ap.rearrange("p (e i) -> p e i", e=E)

            t = dve.do([t], V.tensor_scalar, g3(cnt), ei(b_.t[:, 256:512]), float(D), None, ALU.mult)
            t = dve.do([t, t_part], V.tensor_tensor_scan, inc, part, cnt, 0.0, ALU.mult, ALU.add)
            last = g3(inc)[:, :, E - 1]
            t = dve.do([t], V.tensor_scalar, e_u[:, 0:16], last, 127.0, None, ALU.add)
            t = dve.do([t], V.tensor_scalar, e_u[:, 16:32], e_u[:, 0:16], 7, None, ALU.logical_shift_right)
            t = dve.do([t], V.tensor_copy, e_n[:, 0:16], e_u[:, 16:32])
            t = dve.do([t], V.tensor_tensor_scan, e_n[:, 16:32], e_n[:, 0:16], e_n[:, 0:16], 0.0, ALU.add, ALU.bypass)
            t_e = t
            t = dve.do([t], V.tensor_tensor, e_n[:, 32:48], e_n[:, 16:32], e_n[:, 0:16], ALU.subtract)
            t = dve.do([t], V.tensor_tensor, bas, inc, cnt, ALU.subtract)
            t = dve.do([t], V.scalar_tensor_tensor, g3(bas), e_n[:, 32:48, None].broadcast_to([P, E, 16]), 128.0, g3(bas), ALU.mult, ALU.add)
            t = dve.do([t, *s1.free], V.tensor_tensor, g3(pos), ei(b_.t[:, 0:256]), g3(bas), ALU.add)
            b_.done(t)
            yield
            for k in range(2):
                h = s1.t[:, 1, k * 256:(k + 1) * 256].rearrange("p (i e) -> p i e", e=E)
                t1 = dve.do([t], V.tensor_tensor, h, hk[k].rearrange("p (i e) -> p i e", e=E), pos.rearrange("p (e i) -> p i e", e=E), ALU.mult)
                t1 = dve.do([t1], V.tensor_reduce, slot_f[:, 16 * k:16 * k + 16], h, AX, ALU.add)
            t = dve.do([t1], V.tensor_copy, slot_i[:, :], slot_f[:, 0:32])
            t_slot = t
            dve.do([t], V.tensor_scalar, slot_q[:, 0:32], slot_i[:, :], 7, None, ALU.logical_shift_right)
            t = dve.do([], V.tensor_scalar, slot_q[:, 32:64], slot_i[:, :], 127, None, ALU.bitwise_and)
            t = dve.do([t], V.tensor_copy, slot_f[:, :], slot_q[:, :])
            s0.done(t)
            s1.done(t)
            cm = s2.t[0:1, :, :].rearrange("p c t -> p (c t)")[:, 0:TW * E].rearrange("p (j e) -> p j e", e=E)
            t1 = dve.do([t_e, *s2.free], V.tensor_tensor, cm, e_n[0:1, None, 16:32].broadcast_to([1, TW, E]),
                        iota[0:1, 0:TW, None].broadcast_to([1, TW, E]), ALU.is_le)
            t1 = dve.do([t1], V.tensor_reduce, slot_g[0:1, :], cm, AX, ALU.add)
            t1 = dve.do([t1], V.tensor_scalar, slot_g[0:1, :], slot_g[0:1, :], float(E - 1), float(EW), ALU.min, ALU.mult)
            state["eoff"] = dve.do([t1], V.tensor_copy, eoff[0:1, :], slot_g[0:1, :])
            yield
            b_ = bank()
            pe.wait(*b_.free)
            s2.done(state["eoff"])
            for g in range(8):
                s = take(*RT)
                bt = s.r[:, 0, :].rearrange("p (n r) -> p n r", r=P)
                at_ = s.r[:, 1, 0:4 * TW].rearrange("p (n j) -> p n j", j=TW)
                t = dve.do([t, *s.free], V.tensor_tensor, at_, iota[:, None, 0:TW].broadcast_to([P, 4, TW]),
                           slot_f[:, 4 * g:4 * g + 4, None].broadcast_to([P, 4, TW]), ALU.is_equal)
                for n in range(4):
                    q = 4 * g + n
                    t = dve.do([], V.tensor_scalar, bt[:, n, :], iota, slot_f[:, 32 + q:33 + q], tokid[:, q % 16:q % 16 + 1], ALU.is_equal, ALU.mult)
                pe.wait(t)
                for n in range(4):
                    q = 4 * g + n
                    t2 = pe.do([], M.matmul, b_.t[:, 0:TW], bt[:, n, :], at_[:, n, :], start=(q == 0), stop=(q == 31))
                s.done(t2)
                if g % 2:
                    yield
            t = dve.do([t2], V.tensor_copy, tab[:, :], b_.t[:, 0:TW])
            b_.done(t)
            state["tab"], state["slot"] = t, t_slot
            yield

        slot_g = put("slot_g", TW)

        def load_experts(a, z, *waits):
            for n in range(a, z):
                s = s_mw[n // 2]
                o = n * EW
                sp.dma(waits, mw[:, o:o + 704], gu[n], s, 2 * (n % 2) + 1)
                state["mw"] = sp.dma([], mw[0:88, o + 704:o + EW], dn[n], s, 2 * (n % 2) + 2)

        y_tok = []

        def moe():
            tiles = [dict() for _ in range(TILES)]
            pe.wait(state["eoff"])

            def fetch_x(j):
                p = take(xg)
                p.turns += 1
                pool.wait(state["tab"], *[state["xn", b] for b in range(NB)], *p.free)
                pool.ops.append(lambda e, p=p, j=j: e.indirect_dma_start(
                    out=p.t[:, :], out_offset=None, in_=xn_d, in_offset=bass.IndirectOffsetOnAxis(ap=tab[:, j:j + 1], axis=0)).then_inc(p.sem, 16))
                tiles[j]["xg"] = (p, (p.sem, 16 * p.turns))

            def turn_x(j):
                p, t = tiles[j]["xg"]
                b_ = bank()
                pe.wait(t, *b_.free)
                for c in range(2):
                    t = pe.do([], M.transpose, b_.t[:, c * P:(c + 1) * P], p.t[:, c * P:(c + 1) * P], ident)
                p.done(t)
                q = take(m_xt)
                t = act.do([t, *q.free], A.activation, q.t[:, :], b_.t[:, 0:2 * P], ACT.Copy)
                b_.done(t)
                tiles[j]["xt"] = (q, t)

            def up_(j):
                q, t = tiles[j]["xt"]
                b_ = bank()
                pe.wait(t, *b_.free)

                def go(e):
                    r = e.value_load(eoff[0:1, j:j + 1], min_val=0, max_val=(E - 1) * EW)
                    tiles[j]["off"] = r
                    for c in range(2):
                        mm = e.matmul(b_.t[:, 0:352], q.t[:, c * P:(c + 1) * P], mw[:, bass.DynSlice(r + c * 352, 352)], start=(c == 0), stop=(c == 1))
                    mm.then_inc(pe.sem, 1)
                pe.n += 1
                pe.ops.append(go)
                t = pe.now()
                q.done(t)
                h = take(m_h)
                t1 = act.do([t, *h.free], A.activation, h.t[:, :], b_.t[:, 0:176], ACT.Silu)
                t1 = dve.do([t1], V.tensor_tensor, h.t[:, :], h.t[:, :], b_.t[:, 176:352], ALU.mult)
                b_.done(t1)
                tiles[j]["h"] = (h, t1)

            def turn_h(j):
                h, t = tiles[j]["h"]
                b_ = bank()
                pe.wait(t, *b_.free)
                for c in range(2):
                    t = pe.do([], M.transpose, b_.t[0:88, c * P:(c + 1) * P], h.t[:, c * 88:(c + 1) * 88], ident)
                h.done(t)
                q = take(m_ht)
                t = act.do([t, *q.free], A.activation, q.t[:, :], b_.t[0:88, 0:2 * P], ACT.Copy)
                b_.done(t)
                tiles[j]["ht"] = (q, t)

            def down(j):
                q, t = tiles[j]["ht"]
                b_ = bank()
                pe.wait(t, *b_.free)

                def go(e):
                    r = tiles[j]["off"]
                    for c in range(2):
                        mm = e.matmul(b_.t[:, 0:D], q.t[:, c * P:(c + 1) * P], mw[0:88, bass.DynSlice(r + (704 + c * D), D)], start=(c == 0), stop=(c == 1))
                    mm.then_inc(pe.sem, 1)
                pe.n += 1
                pe.ops.append(go)
                t = pe.now()
                q.done(t)
                y = take(m_y)
                y.turns += 1
                t = dve.do([t, *y.free], V.tensor_copy, y.t[:, :], b_.t[:, 0:D])
                b_.done(t)
                t = sp.dma([t], y_d[j * P:(j + 1) * P, :], y.t[:, :], y.sem, y.turns)
                y.done(t)
                y_tok.append(t)

            for j in range(2):
                fetch_x(j)
            for j in range(TILES + 3):
                if j < TILES:
                    turn_x(j)
                if j + 2 < TILES:
                    fetch_x(j + 2)
                if 0 <= j - 2 < TILES:
                    turn_h(j - 2)
                if 0 <= j - 1 < TILES:
                    k = j - 1
                    pe.wait(*experts_here(k))
                    up_(k)
                if 0 <= j - 3 < TILES:
                    down(j - 3)
                yield

        def experts_here(k):
            return [(s, 64) for s in s_mw] if k == 0 else []

        def combine(b):
            got = []
            for i in range(4 * b, 4 * b + 4):
                for k in range(2):
                    n = 2 * (i % 4) + k
                    if n % 4 == 0:
                        p = take(slots, h_slots)
                        got.append(p)
                    o = p.t[:, (n % 4) // 2, (n % 2) * D:(n % 2 + 1) * D]
                    pool.wait(state["slot"], *y_tok, *p.free)
                    s = s_ga[8 * b + n]
                    pool.ops.append(lambda e, o=o, i=i, k=k, s=s: e.indirect_dma_start(
                        out=o, out_offset=None, in_=y_d, in_offset=bass.IndirectOffsetOnAxis(ap=slot_i[:, 16 * k + i:16 * k + i + 1], axis=0)).then_inc(s, 16))
                    state["ga", i, k] = (o, (s, 16))
                yield
            for i in range(4 * b, 4 * b + 4):
                for k in range(2):
                    o, t = state["ga", i, k]
                    t = dve.do([t, state["rows", b]], V.scalar_tensor_tensor, rows_[:, i, :], o, gval[:, 2 * i + k:2 * i + k + 1], rows_[:, i, :], ALU.mult, ALU.add)
                    state["rows", b] = t
                if i % 4 == 1:
                    got[0].done(t)
                yield
            got[1].done(t)
            state["out", b] = sp.dma([t], out[b].rearrange("(i p) d -> p i d", p=P), rows_[:, 4 * b:4 * b + 4, :], s_out[b], 1)

        prepared, t_wdu = {}, [None]

        def prep():
            n = 0
            for name, ap, words in (("wsg", wsg, 4096), ("wout", wout, 2048), ("sgu", sgu, 1408), ("sdn", sdn, 768)):
                h, l = pairs[name]
                for o in range(0, words, 1024):
                    k = min(1024, words - o)
                    s = take(*FR)
                    st = s.t.rearrange("p c t -> p (c t)")[:, 0:k]
                    t = sp.dma(s.free, st, ap[:, o:o + k], s_st[n], 1)
                    n += 1
                    t1 = act.do([t], A.activation, h[:, o:o + k], st, ACT.Copy)
                    t = pool.do([t1], G.tensor_tensor, l[:, o:o + k], st, h[:, o:o + k].bitcast(F32), ALU.subtract)
                    s.done(t1, t)
                    yield
                prepared[name] = t

        load("cst")
        fetch(0)
        for n in ("vec", "wqkv0", "wc"):
            load(n)
        fetch(1)
        for n in ("wo0", "genes", "wdu", "wqkv1", "gate"):
            load(n)
        t = dve.do([arrived("vec")], V.tensor_scalar, misc[:, 0:1], col(V_TP), 0.1, None, ALU.max)
        t = dve.do([t], V.reciprocal, misc[:, 1:2], misc[:, 0:1])
        t_it = dve.do([t], V.tensor_scalar, misc[:, 2:3], misc[:, 1:2], -1.0, None, ALU.mult)
        it, nit = misc[:, 1:2], misc[:, 2:3]

        def prep_wdu():
            t = pool.do([arrived("wdu")], G.tensor_copy, wdu_r[:, :], w("wdu"))
            t_wdu[0] = dve.do([t], V.tensor_tensor, wdu_r[32:64, :], w("wdu")[32:64, :], wdu_r[32:64, :].bitcast(F32), ALU.subtract)
            yield

        def chain(*gens):
            for g in gens:
                yield from g

        fronts = [front(b, b > 0) for b in range(NB)]
        merge((fronts[0], 1), (chain(prep_wdu(), half(fronts[1])), 1), (prep(), 1))
        fetch(2)
        FR.remove(h_slots)
        merge((dense(0, False), 1), (chain(fronts[1], half(fronts[2])), 4))
        fetch(3)
        merge((dense(1, False), 1), (chain(fronts[2], half(fronts[3])), 4))
        merge((dense(2, False, (0,)), 1), (fronts[3], 3))
        load_experts(0, 12, pe.now(), act.now(), dve.now(), pool.now(), *[state["xn", b] for b in range(NB)])
        merge((dense(2, True, (1,)), 1), (route(), 1))
        load_experts(12, E, pe.now(), act.now(), dve.now(), pool.now())
        merge((dense(3, True, (0,)), 1))
        merge((moe(), 1))
        merge((dense(3, True, (1,)), 1), (chain(combine(0), combine(1), combine(2)), 3))
        merge((combine(3), 1))
        sp.wait(*[state["out", b] for b in range(NB)])

        block = ctx.enter_context(nc.Block())

        @block.sync
        def _(e):
            sp.play(e)

        @block.tensor
        def _(e):
            pe.play(e)

        @block.scalar
        def _(e):
            act.play(e)

        @block.vector
        def _(e):
            dve.play(e)

        @block.gpsimd
        def _(e):
            pool.play(e)


def rows(a, n=P):
    return a.reshape(-1, n, a.shape[-1]).transpose(1, 0, 2).reshape(n, -1)


def kernel(**inputs):
    import numpy as _np
    import concourse.bacc as _bacc
    from concourse import mybir as _mybir
    from concourse.bass_utils import run_bass_kernel_spmd as _run

    a = {k: _np.asarray(v) for k, v in inputs.items()}

    def cols(v):
        return v.reshape(-1, P).T

    n = _np.arange(P)
    cst = _np.zeros((P, CW), _np.float32)
    cst[:, C_LN] = LN_EPS
    cst[:, C_LNR] = LN_EPS * EPS
    cst[:, C_RMS] = EPS
    cst[:, C_ID:C_ID + P] = _np.eye(P)
    cst[:, C_MEAN:C_MEAN + P] = 1.0 / D
    cst[:, C_TRI:C_TRI + P] = n[:, None] < n[None, :]
    cst[:, C_IOTA:C_IOTA + P] = n
    cst[:, C_TOK:C_TOK + 16] = n[:, None] + P * n[None, :16]
    g = a["L0_ffn_genes"]
    wdu = _np.concatenate([a["L0_ffn_Wd"].T, a["L0_ffn_Wu"].T], 1)
    sdn = _np.concatenate([a["L1_ffn_shared_down"], _np.zeros((32, D), _np.float32)], 0)
    arrays = {
        "x": a["L0_attn_x"].transpose(0, 2, 1).reshape(NB, 2, P, T).transpose(0, 2, 1, 3),
        "vec": _np.concatenate([
            cols(a["L0_attn_bq"]), cols(a["L0_attn_bk"]), cols(a["L0_attn_bv"]), cols(a["L0_attn_bo"]), cols(a["L0_ffn_norm_w"]),
            _np.broadcast_to(a["L0_ffn_scale"], (P, 1)), _np.broadcast_to(a["L0_ffn_temperature"], (P, 1))], 1),
        "cst": cst,
        "part_d": _np.broadcast_to((_np.arange(256) % 16 != 0).astype(_np.float32), (P, 256)),
        "wqkv0": rows(_np.concatenate([a["L0_attn_Wq"].T, a["L0_attn_Wk"].T, a["L0_attn_Wv"].T], 1)),
        "wo0": rows(a["L0_attn_Wo"].T),
        "wc": rows(a["L0_ffn_Wc"].T),
        "genes": rows(_np.concatenate([g, g, g], 1)),
        "wdu": _np.concatenate([wdu, wdu, wdu], 0),
        "wqkv1": rows(a["L1_attn_w_qkv"].T),
        "wsg": rows(a["L1_attn_w_swiglu"].T),
        "wout": rows(a["L1_attn_w_out"].T),
        "gate": rows(a["L1_ffn_gate_w"].T),
        "sgu": rows(a["L1_ffn_shared_gate_up"]),
        "sdn": rows(sdn),
        "gu": a["L1_ffn_w_gate_up"].reshape(E, 2, P, 352).transpose(0, 2, 1, 3).reshape(E, P, 704),
        "dn": a["L1_ffn_w_down"].reshape(E, 2, 88, D).transpose(0, 2, 1, 3).reshape(E, 88, 512),
    }
    nc = _bacc.Bacc("TRN2", target_bir_lowering=False, num_devices=1)
    sent, aps = {}, {}
    for k, v in arrays.items():
        v = _np.ascontiguousarray(v)
        sent["in_" + k] = v
        aps[k] = nc.dram_tensor("in_" + k, v.shape, _mybir.dt.from_np(v.dtype), kind="ExternalInput").ap()
    aps["out"] = nc.dram_tensor("out_0", (NB, T, D), _mybir.dt.float32, kind="ExternalOutput").ap()
    build(nc, **aps)
    r = _run(nc, [sent], core_ids=[0])
    return r.results[0]["out_0"]
```
